# Optimizing a Trainium2 kernel written in Bass

```python
import numpy as np
import jax
import jax.numpy as jnp

def _softmax(x, axis=-1):
    return jax.nn.softmax(x, axis=axis)

def _gelu(x):
    return jax.nn.gelu(x, approximate=True)

def _silu(x):
    return jax.nn.silu(x)

def _sigmoid(x):
    return jax.nn.sigmoid(x)

def _layernorm(x, axis=-1, eps=1e-05):
    m = jnp.mean(x, axis=axis, keepdims=True)
    v = jnp.var(x, axis=axis, keepdims=True)
    return (x - m) / jnp.sqrt(v + eps)

def _scatter_add(tgt, idx, src, axis=0):
    return tgt.at[idx].add(src)

def _segment_sum(src, seg, n):
    return jax.ops.segment_sum(src, seg, n)
kernel_name = 'mk_dlrm_tower_d1_rec_r8_ca6f78'

def setup_inputs(seed: int=0):
    np.random.seed(seed)
    _w = jnp.asarray

    def _rec_inputs():
        import jax
        import jax.numpy as jnp
        _tk = jax.random.key(seed)
        ids = jnp.stack([jax.random.randint(jax.random.fold_in(_tk, 200 + f), (2048,), 0, v, jnp.int32) for f, v in enumerate([1000, 12500, 1250, 125000, 1250, 1250, 1250, 1000, 1000, 12500, 1000, 1250, 1250, 1250, 1250, 1000, 1250, 12500, 12500, 1250, 1250, 1250, 1000, 1000, 1250, 1250])], axis=1)
        tbl_0 = 0.05 * jax.random.normal(jax.random.fold_in(_tk, 500 + 0), (1000, 128), jnp.float32)
        tbl_1 = 0.05 * jax.random.normal(jax.random.fold_in(_tk, 500 + 1), (12500, 128), jnp.float32)
        tbl_2 = 0.05 * jax.random.normal(jax.random.fold_in(_tk, 500 + 2), (1250, 128), jnp.float32)
        tbl_3 = 0.05 * jax.random.normal(jax.random.fold_in(_tk, 500 + 3), (125000, 128), jnp.float32)
        tbl_4 = 0.05 * jax.random.normal(jax.random.fold_in(_tk, 500 + 4), (1250, 128), jnp.float32)
        tbl_5 = 0.05 * jax.random.normal(jax.random.fold_in(_tk, 500 + 5), (1250, 128), jnp.float32)
        tbl_6 = 0.05 * jax.random.normal(jax.random.fold_in(_tk, 500 + 6), (1250, 128), jnp.float32)
        tbl_7 = 0.05 * jax.random.normal(jax.random.fold_in(_tk, 500 + 7), (1000, 128), jnp.float32)
        tbl_8 = 0.05 * jax.random.normal(jax.random.fold_in(_tk, 500 + 8), (1000, 128), jnp.float32)
        tbl_9 = 0.05 * jax.random.normal(jax.random.fold_in(_tk, 500 + 9), (12500, 128), jnp.float32)
        tbl_10 = 0.05 * jax.random.normal(jax.random.fold_in(_tk, 500 + 10), (1000, 128), jnp.float32)
        tbl_11 = 0.05 * jax.random.normal(jax.random.fold_in(_tk, 500 + 11), (1250, 128), jnp.float32)
        tbl_12 = 0.05 * jax.random.normal(jax.random.fold_in(_tk, 500 + 12), (1250, 128), jnp.float32)
        tbl_13 = 0.05 * jax.random.normal(jax.random.fold_in(_tk, 500 + 13), (1250, 128), jnp.float32)
        tbl_14 = 0.05 * jax.random.normal(jax.random.fold_in(_tk, 500 + 14), (1250, 128), jnp.float32)
        tbl_15 = 0.05 * jax.random.normal(jax.random.fold_in(_tk, 500 + 15), (1000, 128), jnp.float32)
        tbl_16 = 0.05 * jax.random.normal(jax.random.fold_in(_tk, 500 + 16), (1250, 128), jnp.float32)
        tbl_17 = 0.05 * jax.random.normal(jax.random.fold_in(_tk, 500 + 17), (12500, 128), jnp.float32)
        tbl_18 = 0.05 * jax.random.normal(jax.random.fold_in(_tk, 500 + 18), (12500, 128), jnp.float32)
        tbl_19 = 0.05 * jax.random.normal(jax.random.fold_in(_tk, 500 + 19), (1250, 128), jnp.float32)
        tbl_20 = 0.05 * jax.random.normal(jax.random.fold_in(_tk, 500 + 20), (1250, 128), jnp.float32)
        tbl_21 = 0.05 * jax.random.normal(jax.random.fold_in(_tk, 500 + 21), (1250, 128), jnp.float32)
        tbl_22 = 0.05 * jax.random.normal(jax.random.fold_in(_tk, 500 + 22), (1000, 128), jnp.float32)
        tbl_23 = 0.05 * jax.random.normal(jax.random.fold_in(_tk, 500 + 23), (1000, 128), jnp.float32)
        tbl_24 = 0.05 * jax.random.normal(jax.random.fold_in(_tk, 500 + 24), (1250, 128), jnp.float32)
        tbl_25 = 0.05 * jax.random.normal(jax.random.fold_in(_tk, 500 + 25), (1250, 128), jnp.float32)
        _rk = jax.random.fold_in(_tk, 7)
        r_dense_features = -0.000520686 + 1.00062 * jax.random.normal(jax.random.fold_in(_rk, 101), (2048, 128), jnp.float32)
        W_top1 = 0.0405887 * jax.random.normal(jax.random.fold_in(_tk, 801), (607, 512), jnp.float32)
        W_top2 = 0.0441942 * jax.random.normal(jax.random.fold_in(_tk, 802), (512, 256), jnp.float32)
        W_top3 = 0.0625 * jax.random.normal(jax.random.fold_in(_tk, 803), (256, 1), jnp.float32)
        b_top1 = jnp.zeros((512,), jnp.float32)
        b_top2 = jnp.zeros((256,), jnp.float32)
        return (r_dense_features, ids, tbl_0, tbl_1, tbl_2, tbl_3, tbl_4, tbl_5, tbl_6, tbl_7, tbl_8, tbl_9, tbl_10, tbl_11, tbl_12, tbl_13, tbl_14, tbl_15, tbl_16, tbl_17, tbl_18, tbl_19, tbl_20, tbl_21, tbl_22, tbl_23, tbl_24, tbl_25, W_top1, b_top1, W_top2, b_top2, W_top3)
    r_dense_features, ids, tbl_0, tbl_1, tbl_2, tbl_3, tbl_4, tbl_5, tbl_6, tbl_7, tbl_8, tbl_9, tbl_10, tbl_11, tbl_12, tbl_13, tbl_14, tbl_15, tbl_16, tbl_17, tbl_18, tbl_19, tbl_20, tbl_21, tbl_22, tbl_23, tbl_24, tbl_25, W_top1, b_top1, W_top2, b_top2, W_top3 = _rec_inputs()

    def _L0_rec_setup():
        import jax, jax.numpy as jnp
        import numpy as np
        B, F, D = (2048, 26, 128)
        key = jax.random.key(seed)
        k1, k2 = jax.random.split(key)
        dense_features = jax.random.normal(k1, (B, D), dtype=jnp.float32)
        sparse_values = jax.random.normal(k2, (B, F, D), dtype=jnp.float32)
        return {'dense_features': dense_features, 'sparse_values': sparse_values}
    _L0_rec_all = _L0_rec_setup()
    _L0_rec_in = {k: v for k, v in _L0_rec_all.items() if k in ()}
    del _L0_rec_all
    return {'r_dense_features': r_dense_features, 'ids': ids, 'tbl_0': tbl_0, 'tbl_1': tbl_1, 'tbl_2': tbl_2, 'tbl_3': tbl_3, 'tbl_4': tbl_4, 'tbl_5': tbl_5, 'tbl_6': tbl_6, 'tbl_7': tbl_7, 'tbl_8': tbl_8, 'tbl_9': tbl_9, 'tbl_10': tbl_10, 'tbl_11': tbl_11, 'tbl_12': tbl_12, 'tbl_13': tbl_13, 'tbl_14': tbl_14, 'tbl_15': tbl_15, 'tbl_16': tbl_16, 'tbl_17': tbl_17, 'tbl_18': tbl_18, 'tbl_19': tbl_19, 'tbl_20': tbl_20, 'tbl_21': tbl_21, 'tbl_22': tbl_22, 'tbl_23': tbl_23, 'tbl_24': tbl_24, 'tbl_25': tbl_25, 'W_top1': W_top1, 'b_top1': b_top1, 'W_top2': W_top2, 'b_top2': b_top2, 'W_top3': W_top3}

def reference(r_dense_features, ids, tbl_0, tbl_1, tbl_2, tbl_3, tbl_4, tbl_5, tbl_6, tbl_7, tbl_8, tbl_9, tbl_10, tbl_11, tbl_12, tbl_13, tbl_14, tbl_15, tbl_16, tbl_17, tbl_18, tbl_19, tbl_20, tbl_21, tbl_22, tbl_23, tbl_24, tbl_25, W_top1, b_top1, W_top2, b_top2, W_top3):
    import jax
    import jax.numpy as jnp

    def _L0_rec_ref(dense_features, sparse_values):
        import jax, jax.numpy as jnp
        import numpy as np
        B, F, D = (2048, 26, 128)
        sd = jnp.einsum('bfd,bd->bf', sparse_values, dense_features)
        ss = jnp.einsum('bfd,bgd->bfg', sparse_values, sparse_values)
        iu, ju = jnp.triu_indices(F, k=1)
        pairs = ss[:, iu, ju]
        return jnp.concatenate([dense_features, sd, pairs], axis=1)
    e = jnp.stack([tbl_0[ids[:, 0]], tbl_1[ids[:, 1]], tbl_2[ids[:, 2]], tbl_3[ids[:, 3]], tbl_4[ids[:, 4]], tbl_5[ids[:, 5]], tbl_6[ids[:, 6]], tbl_7[ids[:, 7]], tbl_8[ids[:, 8]], tbl_9[ids[:, 9]], tbl_10[ids[:, 10]], tbl_11[ids[:, 11]], tbl_12[ids[:, 12]], tbl_13[ids[:, 13]], tbl_14[ids[:, 14]], tbl_15[ids[:, 15]], tbl_16[ids[:, 16]], tbl_17[ids[:, 17]], tbl_18[ids[:, 18]], tbl_19[ids[:, 19]], tbl_20[ids[:, 20]], tbl_21[ids[:, 21]], tbl_22[ids[:, 22]], tbl_23[ids[:, 23]], tbl_24[ids[:, 24]], tbl_25[ids[:, 25]]], axis=1)
    z = _L0_rec_ref(r_dense_features, e)
    z = z.reshape(z.shape[0], -1)
    h = jnp.concatenate([z, r_dense_features], axis=1)
    h = jnp.maximum(h @ W_top1 + b_top1, 0.0)
    h = jnp.maximum(h @ W_top2 + b_top2, 0.0)
    y = h @ W_top3
    return y

_drawn_inputs = setup_inputs


def setup_inputs(seed=0):
    import zlib

    import numpy as np

    out = dict(_drawn_inputs(seed))
    spreads = {'b_top1': (0.0, 0.1), 'b_top2': (0.0, 0.1)}
    factors = {}
    for name, (base, spread) in spreads.items():
        noise = np.random.default_rng([zlib.crc32(name.encode()), seed]).standard_normal(out[name].shape)
        drawn = base * np.exp(spread * noise) if base else spread * noise
        out[name] = jnp.asarray(drawn.astype(out[name].dtype))
    for name, factor in factors.items():
        out[name] = (out[name] * factor).astype(out[name].dtype)
    return out
```

```python
from contextlib import ExitStack

import concourse.bass as bass
from concourse import mybir

F32 = mybir.dt.float32
F32R = mybir.dt.float32r
I32 = mybir.dt.int32
ALU = mybir.AluOpType
ACT = mybir.ActivationFunctionType

P = 128
D = 128
QUAD = 32
J = P // QUAD
BANK = 512
BLOCK = 4
E_SLOTS = 2
X_SLOTS = 2
HOT_RING = 4
GATHER_GROUP = 4

ONE_HOT_ROWS = 1000
GROUPS = [4, 4, 4, 3, 1]


def runs(positions):
    out = []
    for i, x in enumerate(positions):
        if out and x == out[-1][1] + out[-1][2]:
            out[-1][2] += 1
        else:
            out.append([i, x, 1])
    return out


def dlrm_kernel(nc, dense, ids, id_columns, tables, w1, b1, w2, b2, w3, out):
    B = dense.shape[0]
    TILES = B // P
    F = len(tables)
    V = F + 1
    PAIRS = V * (V - 1) // 2
    N1, N2 = w2.shape
    M1, M2 = N1 // P, N2 // P
    CH = 3
    PC = PAIRS // CH
    assert PC * CH == PAIRS and PC <= P and sum(GROUPS) == TILES and B == P * TILES

    hot = [f for f in range(F) if tables[f].shape[0] == ONE_HOT_ROWS]
    KR = 125
    KC = ONE_HOT_ROWS // KR
    gathered = [f for f in range(F) if f not in hot]
    arrive = [0] + [f + 1 for f in gathered]
    NG = -(-len(arrive) // GATHER_GROUP)
    members = [arrive[g * GATHER_GROUP:(g + 1) * GATHER_GROUP] for g in range(NG)]
    NH = len(hot)
    BLOCKS = TILES // BLOCK
    XW = P * V
    PAD = QUAD - V

    first_pair = [g * (V - 1) - g * (g - 1) // 2 for g in range(V)]

    g_first = [sum(GROUPS[:g]) for g in range(len(GROUPS))]
    g_last = [g_first[g] + GROUPS[g] - 1 for g in range(len(GROUPS))]
    group_of = [g for g, w in enumerate(GROUPS) for _ in range(w)]

    UNIT_STEPS = NH * KC
    STEPS = BLOCKS * UNIT_STEPS
    UNITS = BLOCKS * NH

    def steps_before(t):
        n, k = divmod(t, BLOCK)
        return min(STEPS, UNIT_STEPS * (n + 1) + UNIT_STEPS * k // BLOCK)

    early = {t: [] for t in range(TILES + 1)}
    late = {t: [] for t in range(TILES + 1)}
    for g, e in enumerate(g_last):
        left = TILES - 1 - e
        if left >= 4:
            early[e + 1].append(("rows", g, None))
            late[e + 1].append(("pairs", g, None))
            early[e + 2].append(("layer1", g, range(0, 2)))
            early[e + 3].append(("layer1", g, range(2, M1)))
            early[e + 4].append(("layer2", g, None))
        else:
            at = min(e + 1, TILES)
            early[at] += [("rows", g, None), ("pairs", g, None), ("layer1", g, range(M1)), ("layer2", g, None)]

    def bank_uses(part, g, arg):
        return {"rows": -(-(V - 1) // J), "pairs": CH, "layer1": len(arg or ()), "layer2": M2 + 1}[part]

    use_at = {}
    n = 0
    for t in range(TILES + 1):
        for part in early[t] + late[t]:
            use_at[(part[0], part[1], part[2])] = n
            n += bank_uses(*part)

    ctx = ExitStack()
    with ctx:
        def sb(name, shape, dt=F32):
            return ctx.enter_context(nc.sbuf_tensor(name, shape, dt))

        def sem(name):
            return ctx.enter_context(nc.semaphore(name))

        ident = sb("ident", [P, P])
        ids_sb = sb("ids_sb", [P, TILES * F], I32)
        row_of_i = sb("row_of_i", [P, KC], I32)
        row_of = sb("row_of", [P, KC])
        rows_in = sb("rows_in", [P, E_SLOTS, len(arrive), D])
        vecs = sb("vecs", [P, X_SLOTS, XW + PAD])
        tab_hi = sb("tab_hi", [P, NH, KC, D], F32R)
        tab_lo = sb("tab_lo", [P, NH, KC, D], F32R)
        id_rows = sb("id_rows", [P, 2, BANK], I32)
        hots = sb("hots", [P, HOT_RING, BANK], F32R)
        picked = sb("picked", [P, 2, NH, BANK])
        gram = sb("gram", [P, V - 1, BLOCK, QUAD])
        pairs_row = sb("pairs_row", [P, J, PAIRS])
        pairs_col = sb("pairs_col", [P, CH, BLOCK, J, QUAD])
        dense_col = sb("dense_col", [P, 2, BLOCK, P])
        w1_dense = sb("w1_dense", [P, 2, N1])
        w1_pairs = sb("w1_pairs", [P, CH, N1])
        w2_sb = sb("w2_sb", [P, M1, N2])
        w3_sb = sb("w3_sb", [P, M2])
        b1_sb = sb("b1_sb", [P, M1])
        b2_sb = sb("b2_sb", [P, M2])
        h1 = sb("h1", [P, M1, BANK])
        h2 = sb("h2", [P, M2, BANK])
        y_sb = sb("y_sb", [P, TILES])
        stage = [h1[:, 2 * s:2 * s + 2, :].rearrange("p a n -> p (a n)")[0:KR, 0:KC * D] for s in range(2)]

        turn_ps = [ctx.enter_context(nc.psum_tensor(f"turn_ps{i}", [P, BANK], F32)) for i in range(2)]
        gram_ps = [ctx.enter_context(nc.psum_tensor(f"gram_ps{i}", [P, BANK], F32)) for i in range(2)]
        mlp_ps = [ctx.enter_context(nc.psum_tensor(f"mlp_ps{i}", [P, BANK], F32)) for i in range(2)]
        pick_ps = ctx.enter_context(nc.psum_tensor("pick_ps", [P, BANK], F32))
        ids_ps = ctx.enter_context(nc.psum_tensor("ids_ps", [P, BANK], F32))

        ids_landed = sem("ids_landed")
        landed = [[sem(f"landed{s}_{g}") for g in range(NG)] for s in range(E_SLOTS)]
        dense_landed = [sem(f"dense_landed{s}") for s in range(E_SLOTS)]
        table_landed = [sem(f"table_landed{s}") for s in range(2)]
        id_rows_landed = [sem(f"id_rows_landed{s}") for s in range(2)]
        weights_landed = sem("weights_landed")
        ident_ready = sem("ident_ready")
        row_of_made = sem("row_of_made")
        row_of_ready = sem("row_of_ready")
        pads_zero = sem("pads_zero")
        w1_added = sem("w1_added")
        table_hi = sem("table_hi")
        table_lo = sem("table_lo")
        turned = sem("turned")
        turn_taken = sem("turn_taken")
        vecs_ready = sem("vecs_ready")
        ids_shown = sem("ids_shown")
        hot_made = sem("hot_made")
        hot_used = sem("hot_used")
        pick_taken = sem("pick_taken")
        gram_done = sem("gram_done")
        gram_taken = sem("gram_taken")
        bank_full = [sem(f"bank_full{i}") for i in range(2)]
        bank_taken = [sem(f"bank_taken{i}") for i in range(2)]
        y_stored = sem("y_stored")

        WEIGHT_LOADS = 2 + CH + 4

        block = ctx.enter_context(nc.Block())

        def h1_use(g, m):
            return next(u + m - a[0] for (name, gg, a), u in use_at.items() if name == "layer1" and gg == g and m in a)

        def wait_taken(eng, number):
            eng.wait_ge(bank_taken[number % 2], number // 2 + 1)

        def slot_vecs(t):
            return vecs[:, t % X_SLOTS, 0:XW].rearrange("p (s v) -> p s v", v=V)

        def unit_ids(u):
            n, i = divmod(u, NH)
            return id_columns[hot[i]:hot[i] + 1, n * BANK:(n + 1) * BANK].to_broadcast([P, BANK])

        def units_shown(t):
            return min(UNITS, -(-min(STEPS, steps_before(t + 1) + HOT_RING) // KC))

        @block.sync
        def _(sp):
            sp.dma_start(ids_sb[:, :], ids.rearrange("(p t) f -> p (t f)", t=TILES)).then_inc(ids_landed, 16)

            def load_dense(t):
                if t >= E_SLOTS:
                    sp.wait_ge(turned, NG * (t - E_SLOTS) + 1)
                sp.dma_start(rows_in[:, t % E_SLOTS, 0, :],
                             dense.rearrange("(p t) d -> t p d", t=TILES)[t]).then_inc(dense_landed[t % E_SLOTS], 16)

            def load_ids(u):
                if u >= 2:
                    sp.wait_ge(ids_shown, u - 1)
                sp.dma_start(id_rows[:, u % 2, :], unit_ids(u)).then_inc(id_rows_landed[u % 2], 16)

            def load_table(i):
                if i >= 2:
                    sp.wait_ge(table_lo, i - 1)
                sp.dma_start(stage[i % 2], tables[hot[i]].rearrange("(p c) d -> p (c d)", c=KC)
                             ).then_inc(table_landed[i % 2], 16)

            load_table(0)
            load_ids(0)
            load_ids(1)
            load_table(1)
            load_dense(0)
            load_dense(1)
            sp.dma_start(w1_dense[:, 0, :], w1[0:D, :]).then_inc(weights_landed, 16)
            sp.dma_start(w1_dense[:, 1, :], w1[D + PAIRS:2 * D + PAIRS, :]).then_inc(weights_landed, 16)
            for c in range(CH):
                sp.dma_start(w1_pairs[0:PC, c, :], w1[D + c * PC:D + (c + 1) * PC, :]).then_inc(weights_landed, 16)
            sp.dma_start(w2_sb[:, :, :], w2.rearrange("(k p) n -> p k n", p=P)).then_inc(weights_landed, 16)
            sp.dma_start(w3_sb[:, :], w3.rearrange("(k p) n -> p (k n)", p=P),
                         allow_slow_non_contiguous=True).then_inc(weights_landed, 16)
            sp.dma_start(b1_sb[:, :], b1.rearrange("(k p) -> p k", p=P),
                         allow_slow_non_contiguous=True).then_inc(weights_landed, 16)
            sp.dma_start(b2_sb[:, :], b2.rearrange("(k p) -> p k", p=P),
                         allow_slow_non_contiguous=True).then_inc(weights_landed, 16)
            for i in range(2, NH):
                load_table(i)
                load_ids(i)
            u = NH
            for t in range(TILES):
                while u < units_shown(t):
                    load_ids(u)
                    u += 1
                if t + E_SLOTS < TILES:
                    load_dense(t + E_SLOTS)
            wait_taken(sp, use_at[("layer2", len(GROUPS) - 1, None)] + M2)
            sp.dma_start(out.rearrange("(p t) n -> p (t n)", t=TILES), y_sb[:, :]).then_inc(y_stored, 16)
            sp.wait_ge(y_stored, 16)

        @block.gpsimd
        def _(pool):
            nc.gpsimd.memset(ident[:, :], 0.0).then_inc(row_of_made, 1)
            pool.wait_ge(row_of_made, 1)
            nc.gpsimd.affine_select(out=ident[:, :], in_=ident[:, :], compare_op=ALU.not_equal, fill=1.0, base=0,
                                    pattern=[[-1, P]], channel_multiplier=1).then_inc(ident_ready, 1)
            nc.gpsimd.iota(row_of_i[:, :], [[1, KC]], base=0, channel_multiplier=KC).then_inc(row_of_made, 1)
            pool.wait_ge(ids_landed, 16)
            for t in range(TILES):
                for g in range(NG):
                    if t >= E_SLOTS:
                        pool.wait_ge(turned, NG * (t - E_SLOTS) + g + 1)
                    for i, pos in enumerate(members[g]):
                        if pos == 0:
                            continue
                        f = pos - 1
                        nc.gpsimd.indirect_dma_start(
                            rows_in[:, t % E_SLOTS, g * GATHER_GROUP + i, :], None, tables[f],
                            bass.IndirectOffsetOnAxis(ap=ids_sb[:, t * F + f:t * F + f + 1], axis=0),
                        ).then_inc(landed[t % E_SLOTS][g], 16)

        @block.tensor
        def _(pe):
            def take_bank(number):
                if number >= 2:
                    wait_taken(pe, number - 2)
                return number % 2

            def turn(t):
                for g in range(NG):
                    k = NG * t + g
                    by_gather = len(members[g]) - (g == 0)
                    pe.wait_ge(landed[t % E_SLOTS][g], 16 * by_gather * (t // E_SLOTS + 1))
                    if g == 0:
                        pe.wait_ge(dense_landed[t % E_SLOTS], 16 * (t // E_SLOTS + 1))
                    if k >= 2:
                        pe.wait_ge(turn_taken, k - 1)
                    for i in range(len(members[g])):
                        mm = nc.tensor.transpose(turn_ps[k % 2][:, i * P:(i + 1) * P],
                                                 rows_in[:, t % E_SLOTS, g * GATHER_GROUP + i, :], ident[:, :])
                    mm.then_inc(turned, 1)

            def pick(s):
                u, c = divmod(s, KC)
                i = u % NH
                if u < NH and c == 0:
                    pe.wait_ge(table_lo, i + 1)
                    pe.wait_ge(table_hi, i + 1)
                if c == 0 and u >= 1:
                    pe.wait_ge(pick_taken, u)
                pe.wait_ge(hot_made, s + 1)
                nc.tensor.matmul(pick_ps[:, :], tab_hi[0:KR, i, c, :], hots[0:KR, s % HOT_RING, :],
                                 start=(c == 0), stop=False)
                nc.tensor.matmul(pick_ps[:, :], tab_lo[0:KR, i, c, :], hots[0:KR, s % HOT_RING, :],
                                 start=False, stop=(c == KC - 1)).then_inc(hot_used, 1)

            def products(t):
                s0, s1 = steps_before(t), steps_before(t + 1)
                pe.wait_ge(vecs_ready, t + 1)
                flat = vecs[:, t % X_SLOTS, :]
                done = 0
                for h in range(2):
                    if t >= 1:
                        pe.wait_ge(gram_taken, 2 * (t - 1) + h + 1)
                    for q in range(QUAD // 2):
                        for j in range(J):
                            s = QUAD * j + QUAD // 2 * h + q
                            mm = nc.tensor.matmul(gram_ps[h][QUAD * j:QUAD * (j + 1), q * V:(q + 1) * V],
                                                  flat[:, s * V:s * V + QUAD], flat[:, s * V:(s + 1) * V],
                                                  start=True, stop=True)
                        if q == QUAD // 2 - 1:
                            mm.then_inc(gram_done, 1)
                        if q % 2 == 1:
                            want = (s1 - s0) * (h * QUAD // 2 + q + 1) // QUAD
                            for s in range(done, want):
                                pick(s0 + s)
                            done = want

            def rows(g, arg, number):
                w = GROUPS[g] * QUAD
                pe.wait_ge(gram_taken, 2 * (g_last[g] + 1))
                for r in range(0, V - 1, J):
                    b = take_bank(number + r // J)
                    for i in range(min(J, V - 1 - r)):
                        mm = nc.tensor.transpose(mlp_ps[b][0:w, i * P:(i + 1) * P],
                                                 gram[:, r + i, 0:GROUPS[g], :].rearrange("p k q -> p (k q)"),
                                                 ident[:, :])
                    mm.then_inc(bank_full[b], 1)

            def pairs(g, arg, number):
                w = GROUPS[g] * QUAD
                wait_taken(pe, use_at[("rows", g, None)] + bank_uses("rows", g, None) - 1)
                for c in range(CH):
                    b = take_bank(number + c)
                    for j in range(J):
                        mm = nc.tensor.transpose(mlp_ps[b][0:PC, j * w:(j + 1) * w],
                                                 pairs_row[0:w, j, c * PC:(c + 1) * PC], ident[0:w, 0:w])
                    mm.then_inc(bank_full[b], 1)

            def layer1(g, chunks, number):
                n = GROUPS[g] * P
                if g == 0 and chunks[0] == 0:
                    pe.wait_ge(w1_added, 1)
                    pe.wait_ge(weights_landed, 16 * WEIGHT_LOADS)
                wait_taken(pe, use_at[("pairs", g, None)] + CH - 1)
                pe.wait_ge(vecs_ready, g_last[g] + 1)
                for m in chunks:
                    b = take_bank(number + m - chunks[0])
                    nc.tensor.matmul(mlp_ps[b][:, 0:n], w1_dense[:, 0, m * P:(m + 1) * P],
                                     dense_col[:, g % 2, 0:GROUPS[g], :].rearrange("p k s -> p (k s)"),
                                     start=True, stop=False)
                    for c in range(CH):
                        mm = nc.tensor.matmul(
                            mlp_ps[b][:, 0:n], w1_pairs[0:PC, c, m * P:(m + 1) * P],
                            pairs_col[0:PC, c, 0:GROUPS[g], :, :].rearrange("p k j q -> p (k j q)"),
                            start=False, stop=(c == CH - 1))
                    mm.then_inc(bank_full[b], 1)

            def layer2(g, arg, number):
                n = GROUPS[g] * P
                for m in range(M2):
                    b = take_bank(number + m)
                    for k in range(M1):
                        if m == 0:
                            wait_taken(pe, h1_use(g, k))
                        mm = nc.tensor.matmul(mlp_ps[b][:, 0:n], w2_sb[:, k, m * P:(m + 1) * P], h1[:, k, 0:n],
                                              start=(k == 0), stop=(k == M1 - 1))
                    mm.then_inc(bank_full[b], 1)
                b = take_bank(number + M2)
                wait_taken(pe, number + M2 - 1)
                for k in range(GROUPS[g]):
                    for m in range(M2):
                        mm = nc.tensor.matmul(mlp_ps[b][:, k:k + 1], h2[:, m, k * P:(k + 1) * P], w3_sb[:, m:m + 1],
                                              start=(m == 0), stop=(m == M2 - 1))
                mm.then_inc(bank_full[b], 1)

            parts = {"rows": rows, "pairs": pairs, "layer1": layer1, "layer2": layer2}

            pe.wait_ge(ident_ready, 1)
            pe.wait_ge(pads_zero, X_SLOTS)
            for s in range(steps_before(0)):
                pick(s)
            for t in range(TILES):
                if t < TILES - 1:
                    turn(t)
                for name, g, arg in early[t]:
                    parts[name](g, arg, use_at[(name, g, arg)])
                if t == TILES - 1:
                    turn(t)
                products(t)
                for name, g, arg in late[t]:
                    parts[name](g, arg, use_at[(name, g, arg)])
            for name, g, arg in early[TILES]:
                parts[name](g, arg, use_at[(name, g, arg)])

        @block.vector
        def _(dve):
            def bank_ready(number):
                dve.wait_ge(bank_full[number % 2], number // 2 + 1)
                return number % 2

            def low_half(i):
                dve.wait_ge(table_landed[i % 2], 16 * (i // 2 + 1))
                dve.wait_ge(table_hi, i + 1)
                nc.vector.tensor_tensor(tab_lo[0:KR, i, :, :].rearrange("p c d -> p (c d)"), stage[i % 2],
                                        tab_hi[0:KR, i, :, :].rearrange("p c d -> p (c d)"),
                                        ALU.subtract).then_inc(table_lo, 1)

            def hot(s):
                u, c = divmod(s, KC)
                if c == 0:
                    if u + 1 < NH:
                        low_half(u + 1)
                    dve.wait_ge(ids_shown, u + 1)
                if s >= HOT_RING:
                    dve.wait_ge(hot_used, s - HOT_RING + 1)
                nc.vector.tensor_scalar(hots[0:KR, s % HOT_RING, :], ids_ps[0:KR, :], row_of[0:KR, c:c + 1], None,
                                        ALU.is_equal).then_inc(hot_made, 1)

            def take_products(t, h):
                g = group_of[t]
                k = t - g_first[g]
                dve.wait_ge(gram_done, 2 * t + h + 1)
                nc.vector.tensor_copy(
                    gram[:, :, k, QUAD // 2 * h:QUAD // 2 * (h + 1)].rearrange("p g q -> p q g"),
                    gram_ps[h][:, 0:QUAD // 2 * V].rearrange("p (q g) -> p q g", g=V)[:, :, 0:V - 1],
                ).then_inc(gram_taken, 1)

            def rows(g, arg, number):
                w = GROUPS[g] * QUAD
                for r in range(0, V - 1, J):
                    b = bank_ready(number + r // J)
                    for i in range(min(J, V - 1 - r)):
                        f = r + i
                        src = mlp_ps[b][0:w, i * P:(i + 1) * P].rearrange("p (j v) -> p j v", j=J)
                        op = nc.vector.tensor_copy(
                            pairs_row[0:w, :, first_pair[f]:first_pair[f] + V - 1 - f], src[:, :, f + 1:V])
                    op.then_inc(bank_taken[b], 1)

            def pairs(g, arg, number):
                w = GROUPS[g]
                for c in range(CH):
                    b = bank_ready(number + c)
                    nc.vector.tensor_copy(
                        pairs_col[0:PC, c, 0:w, :, :].rearrange("p k j q -> p j k q"),
                        mlp_ps[b][0:PC, 0:J * w * QUAD].rearrange("p (j k q) -> p j k q", j=J, q=QUAD),
                    ).then_inc(bank_taken[b], 1)

            parts = {"rows": rows, "pairs": pairs}

            for s in range(X_SLOTS):
                nc.vector.memset(vecs[:, s, XW:XW + PAD], 0.0).then_inc(pads_zero, 1)
            dve.wait_ge(row_of_made, 2)
            nc.vector.tensor_copy(row_of[:, :], row_of_i[:, :]).then_inc(row_of_ready, 1)
            dve.wait_ge(row_of_ready, 1)
            if NH:
                low_half(0)
            made = 0
            for s in range(min(STEPS, steps_before(0) + HOT_RING)):
                hot(s)
                made = s + 1
            for t in range(TILES):
                if t == 0:
                    dve.wait_ge(weights_landed, 16 * WEIGHT_LOADS)
                    nc.vector.tensor_tensor(w1_dense[:, 0, :], w1_dense[:, 0, :], w1_dense[:, 1, :],
                                            ALU.add).then_inc(w1_added, 1)
                for name, g, arg in early[t]:
                    if name in parts:
                        parts[name](g, arg, use_at[(name, g, arg)])
                s1 = min(STEPS, steps_before(t + 1) + HOT_RING)
                half = (made + s1) // 2
                for s in range(made, half):
                    hot(s)
                take_products(t, 0)
                for s in range(half, s1):
                    hot(s)
                take_products(t, 1)
                made = s1
                for name, g, arg in late[t]:
                    if name in parts:
                        parts[name](g, arg, use_at[(name, g, arg)])
            for name, g, arg in early[TILES]:
                if name in parts:
                    parts[name](g, arg, use_at[(name, g, arg)])

        @block.scalar
        def _(act):
            def high_half(i):
                act.wait_ge(table_landed[i % 2], 16 * (i // 2 + 1))
                nc.scalar.copy(tab_hi[0:KR, i, :, :].rearrange("p c d -> p (c d)"), stage[i % 2]).then_inc(table_hi, 1)

            def show_ids(u):
                if u + 1 < NH:
                    high_half(u + 1)
                act.wait_ge(id_rows_landed[u % 2], 16 * (u // 2 + 1))
                if u >= 1:
                    act.wait_ge(hot_made, KC * u)
                nc.scalar.copy(ids_ps[:, :], id_rows[:, u % 2, :]).then_inc(ids_shown, 1)

            def take_pick(u):
                n, i = divmod(u, NH)
                act.wait_ge(hot_used, KC * (u + 1))
                if n >= 2:
                    act.wait_ge(vecs_ready, BLOCK * (n - 1))
                nc.scalar.copy(picked[:, n % 2, i, :], pick_ps[:, :]).then_inc(pick_taken, 1)

            def during(s0, s1):
                for s in range(s0, s1):
                    ahead = s + HOT_RING
                    if ahead % KC == 0 and ahead < STEPS:
                        show_ids(ahead // KC)
                    if s % KC == KC - 1:
                        take_pick(s // KC)

            def take_turned(t):
                g_of, slot = group_of[t], slot_vecs(t)
                if t >= X_SLOTS:
                    act.wait_ge(gram_done, 2 * (t - X_SLOTS + 1))
                for g in range(NG):
                    act.wait_ge(turned, NG * t + g + 1)
                    bank = turn_ps[(NG * t + g) % 2]
                    if g == 0:
                        nc.scalar.copy(dense_col[:, g_of % 2, t - g_first[g_of], :], bank[:, 0:P])
                    for i, pos, n in runs(members[g]):
                        op = nc.scalar.copy(slot[:, :, pos:pos + n].rearrange("p s v -> p v s"),
                                            bank[:, i * P:(i + n) * P].rearrange("p (v s) -> p v s", v=n))
                    op.then_inc(turn_taken, 1)
                n, k = divmod(t, BLOCK)
                act.wait_ge(pick_taken, NH * (n + 1))
                for i, pos, m in runs([f + 1 for f in hot]):
                    op = nc.scalar.copy(slot[:, :, pos:pos + m].rearrange("p s v -> p v s"),
                                        picked[:, n % 2, i:i + m, k * P:(k + 1) * P])
                op.then_inc(vecs_ready, 1)

            def bank_ready(number):
                act.wait_ge(bank_full[number % 2], number // 2 + 1)
                return number % 2

            def layer1(g, chunks, number):
                n = GROUPS[g] * P
                if g == 0 and chunks[0] == 0:
                    act.wait_ge(table_lo, NH)
                    act.wait_ge(weights_landed, 16 * WEIGHT_LOADS)
                for m in chunks:
                    b = bank_ready(number + m - chunks[0])
                    nc.scalar.activation(h1[:, m, 0:n], mlp_ps[b][:, 0:n], ACT.Relu,
                                         bias=b1_sb[:, m:m + 1]).then_inc(bank_taken[b], 1)

            def layer2(g, arg, number):
                n = GROUPS[g] * P
                for m in range(M2):
                    b = bank_ready(number + m)
                    nc.scalar.activation(h2[:, m, 0:n], mlp_ps[b][:, 0:n], ACT.Relu,
                                         bias=b2_sb[:, m:m + 1]).then_inc(bank_taken[b], 1)
                b = bank_ready(number + M2)
                nc.scalar.copy(y_sb[:, g_first[g]:g_first[g] + GROUPS[g]],
                               mlp_ps[b][:, 0:GROUPS[g]]).then_inc(bank_taken[b], 1)

            parts = {"layer1": layer1, "layer2": layer2}

            if NH:
                high_half(0)
                show_ids(0)
            during(0, steps_before(0))
            for t in range(TILES):
                if t < TILES - 1:
                    take_turned(t)
                for name, g, arg in early[t]:
                    if name in parts:
                        parts[name](g, arg, use_at[(name, g, arg)])
                if t == TILES - 1:
                    take_turned(t)
                during(steps_before(t), steps_before(t + 1))
            for name, g, arg in early[TILES]:
                if name in parts:
                    parts[name](g, arg, use_at[(name, g, arg)])


def kernel(**inputs):
    import numpy as np
    import concourse.bacc as bacc
    from concourse.bass_utils import run_bass_kernel_spmd

    nc = bacc.Bacc("TRN2", target_bir_lowering=False, num_devices=1)
    arrays = {}

    def dram_in(name, a):
        a = np.ascontiguousarray(a)
        arrays[name] = a
        return nc.dram_tensor(name, a.shape, mybir.dt.from_np(a.dtype), kind="ExternalInput").ap()

    ids = np.asarray(inputs["ids"])
    B, F = ids.shape
    tiles = B // P
    dense = dram_in("dense", inputs["r_dense_features"])
    ids_ap = dram_in("ids", ids)
    id_columns = dram_in("id_columns", ids.reshape(P, tiles, F).transpose(2, 1, 0).reshape(F, B))
    tables = [dram_in(f"tbl_{f}", inputs[f"tbl_{f}"]) for f in range(F)]
    weights = [dram_in(n, inputs[n]) for n in ("W_top1", "b_top1", "W_top2", "b_top2", "W_top3")]
    out = nc.dram_tensor("y", (B, 1), F32, kind="ExternalOutput").ap()
    dlrm_kernel(nc, dense, ids_ap, id_columns, tables, *weights, out)
    r = run_bass_kernel_spmd(nc, [arrays], core_ids=[0])
    return r.results[0]["y"]
```

```python
from contextlib import ExitStack

import concourse.bass as bass
from concourse import mybir

F32 = mybir.dt.float32
F32R = mybir.dt.float32r
I32 = mybir.dt.int32
ALU = mybir.AluOpType
ACT = mybir.ActivationFunctionType

P = 128
D = 128
QUAD = 32
J = P // QUAD
BANK = 512
BLOCK = 4
E_RING = 10
X_SLOTS = 2
HOT_RING = 4
GATHER_GROUP = 4

HOT_TABLES = [7, 7, 7, 7]
ONE_HOT_ROWS = 1000
GROUPS = [4, 4, 4, 2, 2]


def runs(positions):
    out = []
    for i, x in enumerate(positions):
        if out and x == out[-1][1] + out[-1][2]:
            out[-1][2] += 1
        else:
            out.append([i, x, 1])
    return out


def dlrm_kernel(nc, dense, ids, id_columns, tables, w1, b1, w2, b2, w3, out):
    B = dense.shape[0]
    TILES = B // P
    F = len(tables)
    V = F + 1
    PAIRS = V * (V - 1) // 2
    N1, N2 = w2.shape
    M1, M2 = N1 // P, N2 // P
    CH = 3
    PC = PAIRS // CH
    assert PC * CH == PAIRS and PC <= P and sum(GROUPS) == TILES and B == P * TILES

    hot = [f for f in range(F) if tables[f].shape[0] == ONE_HOT_ROWS]
    KR = 125
    KC = ONE_HOT_ROWS // KR
    NH = max(HOT_TABLES)
    BLOCKS = TILES // BLOCK
    assert len(hot) >= NH == HOT_TABLES[0] and len(HOT_TABLES) == BLOCKS
    units = [(n, i) for n in range(BLOCKS) for i in range(HOT_TABLES[n])]
    units_to = [sum(HOT_TABLES[:n]) for n in range(BLOCKS + 1)]
    UNITS = len(units)
    FIRST = units_to[1]

    members = []
    for t in range(TILES):
        arrive = [0] + [f + 1 for f in range(F) if f not in hot[:HOT_TABLES[t // BLOCK]]]
        members.append([arrive[g:g + GATHER_GROUP] for g in range(0, len(arrive), GATHER_GROUP)])
    group_at = [sum(len(m) for m in members[:t]) for t in range(TILES)]
    ring_rows = [0] * E_RING
    gathers_by = []
    for k, m in enumerate(m for tile in members for m in tile):
        ring_rows[k % E_RING] += len(m) - (0 in m)
        gathers_by.append(ring_rows[k % E_RING])
    XW = P * V
    PAD = QUAD - V

    first_pair = [g * (V - 1) - g * (g - 1) // 2 for g in range(V)]

    g_first = [sum(GROUPS[:g]) for g in range(len(GROUPS))]
    g_last = [g_first[g] + GROUPS[g] - 1 for g in range(len(GROUPS))]
    group_of = [g for g, w in enumerate(GROUPS) for _ in range(w)]

    STEPS = UNITS * KC

    def steps_before(t):
        n, k = divmod(t, BLOCK)
        here, then = units_to[min(n + 1, BLOCKS)] * KC, units_to[min(n + 2, BLOCKS)] * KC
        return here + (then - here) * k // BLOCK

    def mixed(picks, others):
        out = []
        for n, piece in enumerate(others):
            out += [piece] + picks[-(-len(picks) * n // len(others)):-(-len(picks) * (n + 1) // len(others))]
        return out if others else list(picks)

    BURSTS = 4
    TURN_AFTER = [0, 1, 1, 2, 3]
    FILLS = [range(r, min(r + J, V - 1)) for r in range(0, V - 1, J)]
    rows_of = lambda g: [("rows", g, r) for r in FILLS]
    pairs_of = lambda g: [("pairs", g, c) for c in range(CH)]
    layer1_of = lambda g: [("layer1", g, m) for m in range(M1)]
    layer2_of = lambda g: [("layer2", g, m) for m in range(M2)]
    layer3_of = lambda g: [("layer3", g, 0)]
    after = {(t, i): [] for t in range(TILES) for i in range(BURSTS)}
    late = {part: [] for part in ("layer1", "layer2", "layer3")}
    for g, e in enumerate(g_last[:-1]):
        after[e + 1, 0] += rows_of(g)[:4]
        after[e + 1, 1] += rows_of(g)[4:]
        after[e + 1, 2] += pairs_of(g)[:1]
        after[e + 1, 3] += pairs_of(g)[1:]
        layers = layer1_of(g) + layer2_of(g) + layer3_of(g)
        start, end = BURSTS * (e + 2), BURSTS * (g_last[g + 1] + 1) + 2
        for n, part in enumerate(layers):
            t, i = divmod(start + (end - start) * n // len(layers), BURSTS)
            if t < TILES:
                after[t, i].append(part)
            else:
                late[part[0]].append(part)
    g = len(GROUPS) - 1
    at_last = (mixed(late["layer1"], rows_of(g)) + mixed(late["layer2"], pairs_of(g))
               + mixed(late["layer3"], layer1_of(g)) + layer2_of(g) + layer3_of(g))

    def steps_after(t, i):
        s0, s1 = steps_before(t), steps_before(t + 1)
        return min(s1, s0 - (-(s1 - s0) // BURSTS) * (i + 1))

    def between(t, i):
        picks = [("pick", t, s) for s in range(steps_after(t, i - 1), steps_after(t, i))]
        turns = [("turn", t + 1, g) for g in range(len(members[t + 1])) if TURN_AFTER[g] == i] if t + 1 < TILES else []
        return mixed(picks, mixed(after[t, i], turns))

    def at_first():
        out = []
        for s in range(steps_before(0)):
            out.append(("pick", 0, s))
            out += [("turn", 0, g) for g in range(len(members[0]))
                    if s + 1 == steps_before(0) * (4 * len(members[0]) + 6 * (g + 1)) // (10 * len(members[0]))]
        return out

    use_at = {}
    for piece in [x for t in range(TILES) for i in range(BURSTS) for x in after[t, i]] + at_last:
        use_at[piece] = len(use_at)

    ctx = ExitStack()
    with ctx:
        def sb(name, shape, dt=F32):
            return ctx.enter_context(nc.sbuf_tensor(name, shape, dt))

        def sem(name):
            return ctx.enter_context(nc.semaphore(name))

        ident = sb("ident", [P, P])
        ids_sb = sb("ids_sb", [P, TILES * F], I32)
        row_of_i = sb("row_of_i", [P, KC], I32)
        row_of = sb("row_of", [P, KC])
        rows_in = sb("rows_in", [P, E_RING, GATHER_GROUP, D])
        vecs = sb("vecs", [P, X_SLOTS, XW + PAD])
        tab_hi = sb("tab_hi", [P, NH, KC, D], F32R)
        tab_lo = sb("tab_lo", [P, NH, KC, D], F32R)
        id_rows = sb("id_rows", [P, 2, BANK], I32)
        hots = sb("hots", [P, HOT_RING, BANK], F32R)
        picked = sb("picked", [P, 2, NH, BANK])
        gram = sb("gram", [P, V - 1, BLOCK, QUAD])
        pairs_row = sb("pairs_row", [P, J, PAIRS])
        pairs_col = sb("pairs_col", [P, CH, BLOCK, J, QUAD])
        dense_col = sb("dense_col", [P, 3, BLOCK, P])
        w1_dense = sb("w1_dense", [P, 2, N1])
        w1_pairs = sb("w1_pairs", [P, CH, N1])
        w2_sb = sb("w2_sb", [P, M1, N2])
        w3_sb = sb("w3_sb", [P, M2])
        b1_sb = sb("b1_sb", [P, M1])
        b2_sb = sb("b2_sb", [P, M2])
        h1 = sb("h1", [P, M1, BANK])
        h2 = sb("h2", [P, M2, BANK])
        y_sb = sb("y_sb", [P, TILES])
        flat = {"h1": h1[:, :, :].rearrange("p m n -> p (m n)"), "h2": h2[:, :, :].rearrange("p m n -> p (m n)"),
                "gram": gram[:, :, :, :].rearrange("p g k q -> p (g k q)"),
                "pairs_row": pairs_row[:, :, :].rearrange("p j n -> p (j n)")}
        rooms = [("h1", 0), ("h1", 1), ("h2", 0), ("gram", 0), ("gram", 1), ("gram", 2), ("pairs_row", 0)]
        stage = [flat[name][0:KR, n * KC * D:(n + 1) * KC * D] for name, n in rooms]

        turn_ps = ctx.enter_context(nc.psum_tensor("turn_ps", [P, BANK], F32))
        gram_ps = [ctx.enter_context(nc.psum_tensor(f"gram_ps{i}", [P, BANK], F32)) for i in range(2)]
        mlp_ps = [ctx.enter_context(nc.psum_tensor(f"mlp_ps{i}", [P, BANK], F32)) for i in range(2)]
        pick_ps = [ctx.enter_context(nc.psum_tensor(f"pick_ps{i}", [P, BANK], F32)) for i in range(2)]
        ids_ps = ctx.enter_context(nc.psum_tensor("ids_ps", [P, BANK], F32))

        ids_landed = sem("ids_landed")
        landed = [sem(f"landed{s}") for s in range(E_RING)]
        dense_landed = [sem(f"dense_landed{s}") for s in range(2)]
        table_landed = [sem(f"table_landed{i}") for i in range(NH)]
        id_rows_landed = [sem(f"id_rows_landed{s}") for s in range(2)]
        weights_landed = sem("weights_landed")
        ident_ready = sem("ident_ready")
        row_of_made = sem("row_of_made")
        row_of_ready = sem("row_of_ready")
        pads_zero = sem("pads_zero")
        w1_added = sem("w1_added")
        table_hi = sem("table_hi")
        table_lo = sem("table_lo")
        turned = sem("turned")
        turn_taken = sem("turn_taken")
        picks_placed = sem("picks_placed")
        ids_shown = sem("ids_shown")
        hot_made = sem("hot_made")
        hot_used = sem("hot_used")
        pick_taken = sem("pick_taken")
        gram_done = sem("gram_done")
        gram_taken = sem("gram_taken")
        bank_full = [sem(f"bank_full{i}") for i in range(2)]
        bank_taken = [sem(f"bank_taken{i}") for i in range(2)]
        y_stored = sem("y_stored")

        WEIGHT_LOADS = 2 + CH + 4

        block = ctx.enter_context(nc.Block())

        def wait_taken(eng, number):
            eng.wait_ge(bank_taken[number % 2], number // 2 + 1)

        def slot_vecs(t):
            return vecs[:, t % X_SLOTS, 0:XW].rearrange("p (s v) -> p s v", v=V)

        def unit_ids(u):
            n, i = units[u]
            return id_columns[hot[i]:hot[i] + 1, n * BANK:(n + 1) * BANK].to_broadcast([P, BANK])

        def units_shown(t):
            return min(UNITS, -(-min(STEPS, steps_before(t + 1) + HOT_RING) // KC))

        @block.sync
        def _(sp):
            sp.dma_start(ids_sb[:, :], ids.rearrange("(p t) f -> p (t f)", t=TILES)).then_inc(ids_landed, 16)

            def load_dense(t):
                k = group_at[t]
                if k >= E_RING:
                    sp.wait_ge(turned, k - E_RING + 1)
                sp.dma_start(rows_in[:, k % E_RING, 0, :],
                             dense.rearrange("(p t) d -> t p d", t=TILES)[t]).then_inc(dense_landed[t % 2], 16)

            def load_ids(u):
                if u >= 2 and u - 2 < FIRST:
                    sp.wait_ge(hot_made, KC * (u - 1))
                elif u >= 2:
                    sp.wait_ge(ids_shown, u - 2 - FIRST + 1)
                sp.dma_start(id_rows[:, u % 2, :], unit_ids(u)).then_inc(id_rows_landed[u % 2], 16)

            def load_table(i):
                sp.dma_start(stage[i], tables[hot[i]].rearrange("(p c) d -> p (c d)", c=KC)
                             ).then_inc(table_landed[i], 16)

            load_table(0)
            load_ids(0)
            load_ids(1)
            load_table(1)
            load_dense(0)
            for i in range(2, NH):
                load_table(i)
            load_dense(1)
            for u in range(2, FIRST):
                load_ids(u)
            sp.dma_start(w1_dense[:, 0, :], w1[0:D, :]).then_inc(weights_landed, 16)
            sp.dma_start(w1_dense[:, 1, :], w1[D + PAIRS:2 * D + PAIRS, :]).then_inc(weights_landed, 16)
            for c in range(CH):
                sp.dma_start(w1_pairs[0:PC, c, :], w1[D + c * PC:D + (c + 1) * PC, :]).then_inc(weights_landed, 16)
            sp.dma_start(w2_sb[:, :, :], w2.rearrange("(k p) n -> p k n", p=P)).then_inc(weights_landed, 16)
            sp.dma_start(w3_sb[:, :], w3.rearrange("(k p) n -> p (k n)", p=P),
                         allow_slow_non_contiguous=True).then_inc(weights_landed, 16)
            sp.dma_start(b1_sb[:, :], b1.rearrange("(k p) -> p k", p=P),
                         allow_slow_non_contiguous=True).then_inc(weights_landed, 16)
            sp.dma_start(b2_sb[:, :], b2.rearrange("(k p) -> p k", p=P),
                         allow_slow_non_contiguous=True).then_inc(weights_landed, 16)
            u = units_to[1]
            for t in range(TILES):
                while u < units_shown(t):
                    load_ids(u)
                    u += 1
                if t + 2 < TILES:
                    load_dense(t + 2)
            wait_taken(sp, use_at["layer3", len(GROUPS) - 1, 0])
            sp.dma_start(out.rearrange("(p t) n -> p (t n)", t=TILES), y_sb[:, :]).then_inc(y_stored, 16)
            sp.wait_ge(y_stored, 16)

        @block.gpsimd
        def _(pool):
            nc.gpsimd.memset(ident[:, :], 0.0).then_inc(row_of_made, 1)
            pool.wait_ge(row_of_made, 1)
            nc.gpsimd.affine_select(out=ident[:, :], in_=ident[:, :], compare_op=ALU.not_equal, fill=1.0, base=0,
                                    pattern=[[-1, P]], channel_multiplier=1).then_inc(ident_ready, 1)
            nc.gpsimd.iota(row_of_i[:, :], [[1, KC]], base=0, channel_multiplier=KC).then_inc(row_of_made, 1)
            pool.wait_ge(ids_landed, 16)
            for t in range(TILES):
                for g, group in enumerate(members[t]):
                    k = group_at[t] + g
                    if k >= E_RING:
                        pool.wait_ge(turned, k - E_RING + 1)
                    for i, pos in enumerate(group):
                        if pos == 0:
                            continue
                        f = pos - 1
                        nc.gpsimd.indirect_dma_start(
                            rows_in[:, k % E_RING, i, :], None, tables[f],
                            bass.IndirectOffsetOnAxis(ap=ids_sb[:, t * F + f:t * F + f + 1], axis=0),
                        ).then_inc(landed[k % E_RING], 16)

        @block.tensor
        def _(pe):
            def take_bank(number):
                if number >= 2:
                    wait_taken(pe, number - 2)
                return number % 2

            def turn(t, g):
                k = group_at[t] + g
                pe.wait_ge(landed[k % E_RING], 16 * gathers_by[k])
                if g == 0:
                    pe.wait_ge(dense_landed[t % 2], 16 * (t // 2 + 1))
                if k >= 1:
                    pe.wait_ge(turn_taken, k)
                for i in range(len(members[t][g])):
                    mm = nc.tensor.transpose(turn_ps[:, i * P:(i + 1) * P],
                                             rows_in[:, k % E_RING, i, :], ident[:, :])
                mm.then_inc(turned, 1)

            def pick(s):
                u, c = divmod(s, KC)
                i = units[u][1]
                if u < NH and c == 0:
                    pe.wait_ge(table_lo, i + 1)
                    pe.wait_ge(table_hi, i + 1)
                if c == 0 and u >= 2:
                    pe.wait_ge(pick_taken, u - 1)
                pe.wait_ge(hot_made, s + 1)
                nc.tensor.matmul(pick_ps[u % 2][:, :], tab_hi[0:KR, i, c, :], hots[0:KR, s % HOT_RING, :],
                                 start=(c == 0), stop=False)
                nc.tensor.matmul(pick_ps[u % 2][:, :], tab_lo[0:KR, i, c, :], hots[0:KR, s % HOT_RING, :],
                                 start=False, stop=(c == KC - 1)).then_inc(hot_used, 1)

            def products(t, i):
                rows_of_d = vecs[:, t % X_SLOTS, :]
                h, q0 = divmod(i * QUAD // BURSTS, QUAD // 2)
                if i == 0:
                    pe.wait_ge(turn_taken, group_at[t] + len(members[t]))
                    pe.wait_ge(picks_placed, t + 1)
                if t >= 1 and q0 == 0:
                    pe.wait_ge(gram_taken, 2 * (t - 1) + h + 1)
                for q in range(q0, q0 + QUAD // BURSTS):
                    for j in range(J):
                        s = QUAD * j + QUAD // 2 * h + q
                        mm = nc.tensor.matmul(gram_ps[h][QUAD * j:QUAD * (j + 1), q * V:(q + 1) * V],
                                              rows_of_d[:, s * V:s * V + QUAD], rows_of_d[:, s * V:(s + 1) * V],
                                              start=True, stop=True)
                if q == QUAD // 2 - 1:
                    mm.then_inc(gram_done, 1)

            def rows(g, fill):
                w = GROUPS[g] * QUAD
                if fill[0] == 0:
                    pe.wait_ge(gram_taken, 2 * (g_last[g] + 1))
                b = take_bank(use_at["rows", g, fill])
                for i, f in enumerate(fill):
                    mm = nc.tensor.transpose(mlp_ps[b][0:w, i * P:(i + 1) * P],
                                             gram[:, f, 0:GROUPS[g], :].rearrange("p k q -> p (k q)"), ident[:, :])
                mm.then_inc(bank_full[b], 1)

            def pairs(g, c):
                w = GROUPS[g] * QUAD
                if c == 0:
                    wait_taken(pe, use_at["rows", g, FILLS[-1]])
                b = take_bank(use_at["pairs", g, c])
                for j in range(J):
                    mm = nc.tensor.transpose(mlp_ps[b][0:PC, j * w:(j + 1) * w],
                                             pairs_row[0:w, j, c * PC:(c + 1) * PC], ident[0:w, 0:w])
                mm.then_inc(bank_full[b], 1)

            def layer1(g, m):
                n = GROUPS[g] * P
                if g == 0 and m == 0:
                    pe.wait_ge(w1_added, 1)
                    pe.wait_ge(weights_landed, 16 * WEIGHT_LOADS)
                if m == 0:
                    pe.wait_ge(turn_taken, group_at[g_last[g]] + 1)
                    wait_taken(pe, use_at["pairs", g, CH - 1])
                b = take_bank(use_at["layer1", g, m])
                nc.tensor.matmul(mlp_ps[b][:, 0:n], w1_dense[:, 0, m * P:(m + 1) * P],
                                 dense_col[:, g % 3, 0:GROUPS[g], :].rearrange("p k s -> p (k s)"),
                                 start=True, stop=False)
                for c in range(CH):
                    mm = nc.tensor.matmul(
                        mlp_ps[b][:, 0:n], w1_pairs[0:PC, c, m * P:(m + 1) * P],
                        pairs_col[0:PC, c, 0:GROUPS[g], :, :].rearrange("p k j q -> p (k j q)"),
                        start=False, stop=(c == CH - 1))
                mm.then_inc(bank_full[b], 1)

            def layer2(g, m):
                n = GROUPS[g] * P
                b = take_bank(use_at["layer2", g, m])
                for k in range(M1):
                    wait_taken(pe, use_at["layer1", g, k])
                    mm = nc.tensor.matmul(mlp_ps[b][:, 0:n], w2_sb[:, k, m * P:(m + 1) * P], h1[:, k, 0:n],
                                          start=(k == 0), stop=(k == M1 - 1))
                mm.then_inc(bank_full[b], 1)

            def layer3(g, _):
                b = take_bank(use_at["layer3", g, 0])
                for m in range(M2):
                    wait_taken(pe, use_at["layer2", g, m])
                for k in range(GROUPS[g]):
                    for m in range(M2):
                        mm = nc.tensor.matmul(mlp_ps[b][:, k:k + 1], h2[:, m, k * P:(k + 1) * P], w3_sb[:, m:m + 1],
                                              start=(m == 0), stop=(m == M2 - 1))
                mm.then_inc(bank_full[b], 1)

            share = {"pick": lambda t, s: pick(s), "turn": turn, "rows": rows, "pairs": pairs, "layer1": layer1,
                     "layer2": layer2, "layer3": layer3}

            pe.wait_ge(ident_ready, 1)
            pe.wait_ge(pads_zero, X_SLOTS)
            for name, x, y in at_first():
                share[name](x, y)
            for t in range(TILES):
                for i in range(BURSTS):
                    products(t, i)
                    for name, x, y in between(t, i):
                        share[name](x, y)
            for name, x, y in at_last:
                share[name](x, y)

        @block.vector
        def _(dve):
            def bank_ready(number):
                dve.wait_ge(bank_full[number % 2], number // 2 + 1)
                return number % 2

            def low_half(i):
                dve.wait_ge(table_landed[i], 16)
                dve.wait_ge(table_hi, i + 1)
                nc.vector.tensor_tensor(tab_lo[0:KR, i, :, :].rearrange("p c d -> p (c d)"), stage[i],
                                        tab_hi[0:KR, i, :, :].rearrange("p c d -> p (c d)"),
                                        ALU.subtract).then_inc(table_lo, 1)

            def hot(s):
                u, c = divmod(s, KC)
                if c == 0:
                    if u < FIRST:
                        dve.wait_ge(id_rows_landed[u % 2], 16 * (u // 2 + 1))
                    else:
                        dve.wait_ge(ids_shown, u - FIRST + 1)
                if c == HOT_RING and u + 1 < NH:
                    low_half(u + 1)
                if s >= HOT_RING:
                    dve.wait_ge(hot_used, s - HOT_RING + 1)
                shown = id_rows[0:KR, u % 2, :] if u < FIRST else ids_ps[0:KR, :]
                nc.vector.tensor_scalar(hots[0:KR, s % HOT_RING, :], shown, row_of[0:KR, c:c + 1], None,
                                        ALU.is_equal).then_inc(hot_made, 1)

            def take_products(t, h):
                g = group_of[t]
                k = t - g_first[g]
                dve.wait_ge(gram_done, 2 * t + h + 1)
                nc.vector.tensor_copy(
                    gram[:, :, k, QUAD // 2 * h:QUAD // 2 * (h + 1)].rearrange("p g q -> p q g"),
                    gram_ps[h][:, 0:QUAD // 2 * V].rearrange("p (q g) -> p q g", g=V)[:, :, 0:V - 1],
                ).then_inc(gram_taken, 1)

            def rows(g, fill):
                w = GROUPS[g] * QUAD
                b = bank_ready(use_at["rows", g, fill])
                for i, f in enumerate(fill):
                    src = mlp_ps[b][0:w, i * P:(i + 1) * P].rearrange("p (j v) -> p j v", j=J)
                    op = nc.vector.tensor_copy(
                        pairs_row[0:w, :, first_pair[f]:first_pair[f] + V - 1 - f], src[:, :, f + 1:V])
                op.then_inc(bank_taken[b], 1)

            def pairs(g, c):
                w = GROUPS[g]
                b = bank_ready(use_at["pairs", g, c])
                nc.vector.tensor_copy(
                    pairs_col[0:PC, c, 0:w, :, :].rearrange("p k j q -> p j k q"),
                    mlp_ps[b][0:PC, 0:J * w * QUAD].rearrange("p (j k q) -> p j k q", j=J, q=QUAD),
                ).then_inc(bank_taken[b], 1)

            def pick(t, s):
                if s + HOT_RING < STEPS:
                    hot(s + HOT_RING)

            share = {"pick": pick, "rows": rows, "pairs": pairs}

            def do_share(pieces):
                for name, x, y in pieces:
                    if name in share:
                        share[name](x, y)

            for s in range(X_SLOTS):
                nc.vector.memset(vecs[:, s, XW:XW + PAD], 0.0).then_inc(pads_zero, 1)
            dve.wait_ge(row_of_made, 2)
            nc.vector.tensor_copy(row_of[:, :], row_of_i[:, :]).then_inc(row_of_ready, 1)
            dve.wait_ge(row_of_ready, 1)
            low_half(0)
            for s in range(HOT_RING):
                hot(s)
            do_share(at_first())
            for t in range(TILES):
                if t == 2:
                    dve.wait_ge(weights_landed, 16 * WEIGHT_LOADS)
                    nc.vector.tensor_tensor(w1_dense[:, 0, :], w1_dense[:, 0, :], w1_dense[:, 1, :],
                                            ALU.add).then_inc(w1_added, 1)
                for i in range(BURSTS):
                    do_share(between(t, i))
                    if (i + 1) % (BURSTS // 2) == 0:
                        take_products(t, i // (BURSTS // 2))
            do_share(at_last)

        @block.scalar
        def _(act):
            def high_half(i):
                act.wait_ge(table_landed[i], 16)
                nc.scalar.copy(tab_hi[0:KR, i, :, :].rearrange("p c d -> p (c d)"), stage[i]).then_inc(table_hi, 1)

            def show_ids(u):
                act.wait_ge(id_rows_landed[u % 2], 16 * (u // 2 + 1))
                act.wait_ge(hot_made, KC * u)
                nc.scalar.copy(ids_ps[:, :], id_rows[:, u % 2, :]).then_inc(ids_shown, 1)

            def take_pick(u):
                n, i = units[u]
                act.wait_ge(hot_used, KC * (u + 1))
                if n >= 2:
                    act.wait_ge(picks_placed, BLOCK * (n - 1))
                nc.scalar.copy(picked[:, n % 2, i, :], pick_ps[u % 2][:, :]).then_inc(pick_taken, 1)

            def pick(t, s):
                ahead = s + HOT_RING
                u, c = divmod(s, KC)
                if ahead % KC == 0 and FIRST * KC <= ahead < STEPS:
                    show_ids(ahead // KC)
                if c == KC - 1:
                    take_pick(u)
                    if u < FIRST - 1:
                        place_picked(0, range(u, u + 1))
                if c == 0 and u + 2 < NH:
                    high_half(u + 2)

            def take_turned(t, g):
                g_of, slot = group_of[t], slot_vecs(t)
                if t >= X_SLOTS and g == 0:
                    act.wait_ge(gram_done, 2 * (t - X_SLOTS + 1))
                act.wait_ge(turned, group_at[t] + g + 1)
                if g == 0:
                    nc.scalar.copy(dense_col[:, g_of % 3, t - g_first[g_of], :], turn_ps[:, 0:P])
                for i, pos, n in runs(members[t][g]):
                    op = nc.scalar.copy(slot[:, :, pos:pos + n].rearrange("p s v -> p v s"),
                                        turn_ps[:, i * P:(i + n) * P].rearrange("p (v s) -> p v s", v=n))
                op.then_inc(turn_taken, 1)

            def place_picked(t, which):
                n, k = divmod(t, BLOCK)
                if not which:
                    return
                act.wait_ge(pick_taken, units_to[n] + which[-1] + 1)
                for i, pos, m in runs([hot[i] + 1 for i in which]):
                    i += which[0]
                    op = nc.scalar.copy(slot_vecs(t)[:, :, pos:pos + m].rearrange("p s v -> p v s"),
                                        picked[:, n % 2, i:i + m, k * P:(k + 1) * P])
                if which[-1] == HOT_TABLES[n] - 1:
                    op.then_inc(picks_placed, 1)

            def bank_ready(number):
                act.wait_ge(bank_full[number % 2], number // 2 + 1)
                return number % 2

            def layer1(g, m):
                n = GROUPS[g] * P
                if g == 0 and m == 0:
                    act.wait_ge(table_lo, NH)
                    act.wait_ge(weights_landed, 16 * WEIGHT_LOADS)
                b = bank_ready(use_at["layer1", g, m])
                nc.scalar.activation(h1[:, m, 0:n], mlp_ps[b][:, 0:n], ACT.Relu,
                                     bias=b1_sb[:, m:m + 1]).then_inc(bank_taken[b], 1)

            def layer2(g, m):
                n = GROUPS[g] * P
                b = bank_ready(use_at["layer2", g, m])
                nc.scalar.activation(h2[:, m, 0:n], mlp_ps[b][:, 0:n], ACT.Relu,
                                     bias=b2_sb[:, m:m + 1]).then_inc(bank_taken[b], 1)

            def layer3(g, _):
                b = bank_ready(use_at["layer3", g, 0])
                nc.scalar.copy(y_sb[:, g_first[g]:g_first[g] + GROUPS[g]],
                               mlp_ps[b][:, 0:GROUPS[g]]).then_inc(bank_taken[b], 1)

            share = {"pick": pick, "turn": take_turned, "layer1": layer1, "layer2": layer2, "layer3": layer3}

            def do_share(pieces):
                for name, x, y in pieces:
                    if name in share:
                        share[name](x, y)

            high_half(0)
            high_half(1)
            do_share(at_first())
            place_picked(0, range(FIRST - 1, FIRST))
            for t in range(TILES):
                placed = 0
                for i in range(BURSTS):
                    do_share(between(t, i))
                    if i >= BURSTS - 2 and t + 1 < TILES:
                        n, k = divmod(t + 1, BLOCK)
                        done = HOT_TABLES[n] if k else steps_after(t, i) // KC - units_to[n]
                        place_picked(t + 1, range(placed, done))
                        placed = done
            do_share(at_last)


def kernel(**inputs):
    import numpy as np
    import concourse.bacc as bacc
    from concourse.bass_utils import run_bass_kernel_spmd

    nc = bacc.Bacc("TRN2", target_bir_lowering=False, num_devices=1)
    arrays = {}

    def dram_in(name, a):
        a = np.ascontiguousarray(a)
        arrays[name] = a
        return nc.dram_tensor(name, a.shape, mybir.dt.from_np(a.dtype), kind="ExternalInput").ap()

    ids = np.asarray(inputs["ids"])
    B, F = ids.shape
    tiles = B // P
    dense = dram_in("dense", inputs["r_dense_features"])
    ids_ap = dram_in("ids", ids)
    id_columns = dram_in("id_columns", ids.reshape(P, tiles, F).transpose(2, 1, 0).reshape(F, B))
    tables = [dram_in(f"tbl_{f}", inputs[f"tbl_{f}"]) for f in range(F)]
    weights = [dram_in(n, inputs[n]) for n in ("W_top1", "b_top1", "W_top2", "b_top2", "W_top3")]
    out = nc.dram_tensor("y", (B, 1), F32, kind="ExternalOutput").ap()
    dlrm_kernel(nc, dense, ids_ap, id_columns, tables, *weights, out)
    r = run_bass_kernel_spmd(nc, [arrays], core_ids=[0])
    return r.results[0]["y"]
```
